# Optimizing a Trainium2 kernel written in Bass

```python
import numpy as np
import jax
import jax.numpy as jnp

def _softmax(x, axis=-1):
    return jax.nn.softmax(x, axis=axis)

def _gelu(x):
    return jax.nn.gelu(x, approximate=True)

def _silu(x):
    return jax.nn.silu(x)

def _sigmoid(x):
    return jax.nn.sigmoid(x)

def _layernorm(x, axis=-1, eps=1e-05):
    m = jnp.mean(x, axis=axis, keepdims=True)
    v = jnp.var(x, axis=axis, keepdims=True)
    return (x - m) / jnp.sqrt(v + eps)

def _scatter_add(tgt, idx, src, axis=0):
    return tgt.at[idx].add(src)

def _segment_sum(src, seg, n):
    return jax.ops.segment_sum(src, seg, n)
kernel_name = 'mk_adaln_d2_jaxref_r8_c328ae'

def setup_inputs(seed: int=0):
    np.random.seed(seed)
    _w = jnp.asarray

    def _L0_attn_setup():
        import jax, jax.numpy as jnp
        import numpy as np
        B, S, D = (2, 256, 128)
        H = 16
        HD = D // H
        WINDOW = 128
        SCALE = HD ** (-0.5)

        def _local_mask(seq_len):
            idx = jnp.arange(seq_len)
            band = jnp.abs(idx[:, None] - idx[None, :]) <= WINDOW // 2
            return jnp.where(band, 0.0, -jnp.inf).astype(jnp.float32)
        key = jax.random.key(seed)
        ks = jax.random.split(key, 5)
        x = jax.random.normal(ks[0], (B, S, D), dtype=jnp.float32)
        w_qkv = jax.random.normal(ks[1], (D, 3 * D), dtype=jnp.float32) * D ** (-0.5)
        b_qkv = jax.random.normal(ks[2], (3 * D,), dtype=jnp.float32) * 0.02
        w_out = jax.random.normal(ks[3], (D, D), dtype=jnp.float32) * D ** (-0.5)
        b_out = jax.random.normal(ks[4], (D,), dtype=jnp.float32) * 0.02
        return {'x': x, 'w_qkv': w_qkv, 'b_qkv': b_qkv, 'w_out': w_out, 'b_out': b_out}
    _L0_attn_in = _L0_attn_setup()

    def _L0_ffn_setup():
        import jax, jax.numpy as jnp
        import numpy as np
        E = 8
        TOPK = 2

        def _moe_forward(x, Wg, W1, W2, W3):
            B, S, D = x.shape
            xt = x.reshape(-1, D)
            T = xt.shape[0]
            logits = xt @ Wg.T
            scores = jax.nn.softmax(logits, axis=-1)
            w, idx = jax.lax.top_k(scores, TOPK)
            w = w / (w.sum(axis=-1, keepdims=True) + 1e-20)
            cw = jnp.zeros((T, E), xt.dtype).at[jnp.arange(T)[:, None], idx].add(w)
            h = jax.nn.silu(jnp.einsum('td,ehd->teh', xt, W1)) * jnp.einsum('td,ehd->teh', xt, W3)
            out = jnp.einsum('teh,edh->ted', h, W2)
            y = jnp.einsum('te,ted->td', cw, out)
            return y.reshape(B, S, D)
        key = jax.random.key(seed)
        k0, k1, k2, k3, k4 = jax.random.split(key, 5)
        B, S, D, H = (1, 256, 128, 352)
        scale = 0.02
        x = jax.random.normal(k0, (B, S, D), jnp.float32)
        Wg = jax.random.normal(k1, (E, D), jnp.float32) * scale
        W1 = jax.random.normal(k2, (E, H, D), jnp.float32) * scale
        W2 = jax.random.normal(k3, (E, D, H), jnp.float32) * scale
        W3 = jax.random.normal(k4, (E, H, D), jnp.float32) * scale
        return {'x': x, 'Wg': Wg, 'W1': W1, 'W2': W2, 'W3': W3}
    _L0_ffn_in = _L0_ffn_setup()
    _L0_c = _w((lambda *s: np.random.randn(*s).astype(np.float32) * 0.05)(32, 128))
    _L0_wmod = _w((lambda *s: np.random.randn(*s).astype(np.float32) * 0.05)(128, 6 * 128) * 128 ** (-0.5))

    def _L1_attn_setup():
        import jax, jax.numpy as jnp
        import numpy as np
        NUM_BLOCKS = 8
        D = 128
        FF = 512
        B, S = (4, 512)
        EPS_ATTN = 1e-06
        EPS_LN = 1e-06

        def _ln(x, scale, bias):
            m = jnp.mean(x, axis=-1, keepdims=True)
            v = jnp.var(x, axis=-1, keepdims=True)
            return (x - m) * jax.lax.rsqrt(v + EPS_LN) * scale + bias

        def _forward(x, Wq, bq, Wk, bk, Wv, bv, Wo, bo, ln1_s, ln1_b, W1, b1, W2, b2, ln2_s, ln2_b):
            gelu = lambda t: jax.nn.gelu(t, approximate=True)
            fmap = lambda t: jax.nn.elu(t) + 1.0
            for i in range(NUM_BLOCKS):
                residual = x
                Q = fmap(x @ Wq[i] + bq[i])
                K = fmap(x @ Wk[i] + bk[i])
                value = x @ Wv[i] + bv[i]
                KV = jnp.einsum('nsh,nsh->nh', K, value)
                Ksum = jnp.sum(K, axis=1)
                Z = 1.0 / (Q * Ksum[:, None, :] + EPS_ATTN)
                V = Q * KV[:, None, :] * Z
                attn_out = gelu(V @ Wo[i] + bo[i])
                x = _ln(attn_out + residual, ln1_s[i], ln1_b[i])
                residual = x
                h = gelu(x @ W1[i] + b1[i])
                ff_out = gelu(h @ W2[i] + b2[i])
                x = _ln(ff_out + residual, ln2_s[i], ln2_b[i])
            return x
        key = jax.random.key(seed)
        ks = jax.random.split(key, 16)
        g = lambda k, shape, fan: jax.random.normal(k, shape, jnp.float32) * (1.0 / np.sqrt(fan))
        inp = {'x': jax.random.normal(ks[0], (B, S, D), jnp.float32), 'Wq': g(ks[1], (NUM_BLOCKS, D, D), D), 'bq': jnp.zeros((NUM_BLOCKS, D), jnp.float32), 'Wk': g(ks[2], (NUM_BLOCKS, D, D), D), 'bk': jnp.zeros((NUM_BLOCKS, D), jnp.float32), 'Wv': g(ks[3], (NUM_BLOCKS, D, D), D), 'bv': jnp.zeros((NUM_BLOCKS, D), jnp.float32), 'Wo': g(ks[4], (NUM_BLOCKS, D, D), D), 'bo': jnp.zeros((NUM_BLOCKS, D), jnp.float32), 'ln1_s': jnp.ones((NUM_BLOCKS, D), jnp.float32), 'ln1_b': jnp.zeros((NUM_BLOCKS, D), jnp.float32), 'W1': g(ks[5], (NUM_BLOCKS, D, FF), D), 'b1': jnp.zeros((NUM_BLOCKS, FF), jnp.float32), 'W2': g(ks[6], (NUM_BLOCKS, FF, D), FF), 'b2': jnp.zeros((NUM_BLOCKS, D), jnp.float32), 'ln2_s': jnp.ones((NUM_BLOCKS, D), jnp.float32), 'ln2_b': jnp.zeros((NUM_BLOCKS, D), jnp.float32)}
        return inp
    _L1_attn_in = _L1_attn_setup()

    def _L1_ffn_setup():
        import jax, jax.numpy as jnp
        import numpy as np
        ALPHA = 1.0
        key = jax.random.key(seed)
        ks = jax.random.split(key, 7)
        B, S, IN, OUT = (8, 1024, 128, 128)
        RANK, DDIM, UDIM = (4, 100, 50)
        return {'hidden_states': jax.random.normal(ks[0], (B, S, IN), dtype=jnp.float32), 'W': jax.random.normal(ks[1], (OUT, IN), dtype=jnp.float32) * 0.02, 'b': jax.random.normal(ks[2], (OUT,), dtype=jnp.float32) * 0.02, 'lora_down': jax.random.normal(ks[3], (RANK, DDIM), dtype=jnp.float32) * 0.1, 'lora_up': jax.random.normal(ks[4], (UDIM, RANK), dtype=jnp.float32) * 0.1, 'down_aux': jax.random.normal(ks[5], (DDIM, IN), dtype=jnp.float32) * 0.03, 'up_aux': jax.random.normal(ks[6], (OUT, UDIM), dtype=jnp.float32) * 0.03}
    _L1_ffn_in = _L1_ffn_setup()
    _L1_c = _w((lambda *s: np.random.randn(*s).astype(np.float32) * 0.05)(32, 128))
    _L1_wmod = _w((lambda *s: np.random.randn(*s).astype(np.float32) * 0.05)(128, 6 * 128) * 128 ** (-0.5))
    _d = {'L0_attn_x': _L0_attn_in['x'], 'L0_attn_w_qkv': _L0_attn_in['w_qkv'], 'L0_attn_b_qkv': _L0_attn_in['b_qkv'], 'L0_attn_w_out': _L0_attn_in['w_out'], 'L0_attn_b_out': _L0_attn_in['b_out'], 'L0_ffn_Wg': _L0_ffn_in['Wg'], 'L0_ffn_W1': _L0_ffn_in['W1'], 'L0_ffn_W2': _L0_ffn_in['W2'], 'L0_ffn_W3': _L0_ffn_in['W3'], 'L0_c': _L0_c, 'L0_wmod': _L0_wmod, 'L1_attn_Wq': _L1_attn_in['Wq'], 'L1_attn_bq': _L1_attn_in['bq'], 'L1_attn_Wk': _L1_attn_in['Wk'], 'L1_attn_bk': _L1_attn_in['bk'], 'L1_attn_Wv': _L1_attn_in['Wv'], 'L1_attn_bv': _L1_attn_in['bv'], 'L1_attn_Wo': _L1_attn_in['Wo'], 'L1_attn_bo': _L1_attn_in['bo'], 'L1_attn_ln1_s': _L1_attn_in['ln1_s'], 'L1_attn_ln1_b': _L1_attn_in['ln1_b'], 'L1_attn_W1': _L1_attn_in['W1'], 'L1_attn_b1': _L1_attn_in['b1'], 'L1_attn_W2': _L1_attn_in['W2'], 'L1_attn_b2': _L1_attn_in['b2'], 'L1_attn_ln2_s': _L1_attn_in['ln2_s'], 'L1_attn_ln2_b': _L1_attn_in['ln2_b'], 'L1_ffn_W': _L1_ffn_in['W'], 'L1_ffn_b': _L1_ffn_in['b'], 'L1_ffn_lora_down': _L1_ffn_in['lora_down'], 'L1_ffn_lora_up': _L1_ffn_in['lora_up'], 'L1_ffn_down_aux': _L1_ffn_in['down_aux'], 'L1_ffn_up_aux': _L1_ffn_in['up_aux'], 'L1_c': _L1_c, 'L1_wmod': _L1_wmod}
    _x0 = _d['L0_attn_x']
    _d['L0_attn_x'] = jax.random.normal(jax.random.fold_in(jax.random.key(seed), 1), (32, 256, 128), dtype=_x0.dtype)
    del _x0
    return _d

def reference(L0_attn_x, L0_attn_w_qkv, L0_attn_b_qkv, L0_attn_w_out, L0_attn_b_out, L0_ffn_Wg, L0_ffn_W1, L0_ffn_W2, L0_ffn_W3, L0_c, L0_wmod, L1_attn_Wq, L1_attn_bq, L1_attn_Wk, L1_attn_bk, L1_attn_Wv, L1_attn_bv, L1_attn_Wo, L1_attn_bo, L1_attn_ln1_s, L1_attn_ln1_b, L1_attn_W1, L1_attn_b1, L1_attn_W2, L1_attn_b2, L1_attn_ln2_s, L1_attn_ln2_b, L1_ffn_W, L1_ffn_b, L1_ffn_lora_down, L1_ffn_lora_up, L1_ffn_down_aux, L1_ffn_up_aux, L1_c, L1_wmod):

    def _L0_attn_ref(x, w_qkv, b_qkv, w_out, b_out):
        import jax, jax.numpy as jnp
        import numpy as np
        B, S, D = (2, 256, 128)
        H = 16
        HD = D // H
        WINDOW = 128
        SCALE = HD ** (-0.5)

        def _local_mask(seq_len):
            idx = jnp.arange(seq_len)
            band = jnp.abs(idx[:, None] - idx[None, :]) <= WINDOW // 2
            return jnp.where(band, 0.0, -jnp.inf).astype(jnp.float32)
        b, s, _ = x.shape
        qkv = x @ w_qkv + b_qkv
        qkv = qkv.reshape(b, s, 3, H, HD).transpose(2, 0, 3, 1, 4)
        q, k, v = (qkv[0], qkv[1], qkv[2])
        mask = _local_mask(s)
        scores = jnp.einsum('bhqd,bhkd->bhqk', q, k) * SCALE + mask
        attn = jax.nn.softmax(scores, axis=-1)
        out = jnp.einsum('bhqk,bhkd->bhqd', attn, v)
        out = out.transpose(0, 2, 1, 3).reshape(b, s, D)
        return out @ w_out + b_out

    def _L0_ffn_ref(x, Wg, W1, W2, W3):
        import jax, jax.numpy as jnp
        import numpy as np
        E = 8
        TOPK = 2

        def _moe_forward(x, Wg, W1, W2, W3):
            B, S, D = x.shape
            xt = x.reshape(-1, D)
            T = xt.shape[0]
            logits = xt @ Wg.T
            scores = jax.nn.softmax(logits, axis=-1)
            w, idx = jax.lax.top_k(scores, TOPK)
            w = w / (w.sum(axis=-1, keepdims=True) + 1e-20)
            cw = jnp.zeros((T, E), xt.dtype).at[jnp.arange(T)[:, None], idx].add(w)
            h = jax.nn.silu(jnp.einsum('td,ehd->teh', xt, W1)) * jnp.einsum('td,ehd->teh', xt, W3)
            out = jnp.einsum('teh,edh->ted', h, W2)
            y = jnp.einsum('te,ted->td', cw, out)
            return y.reshape(B, S, D)
        return _moe_forward(x, Wg, W1, W2, W3)

    def _L1_attn_ref(x, Wq, bq, Wk, bk, Wv, bv, Wo, bo, ln1_s, ln1_b, W1, b1, W2, b2, ln2_s, ln2_b):
        import jax, jax.numpy as jnp
        import numpy as np
        NUM_BLOCKS = 8
        D = 128
        FF = 512
        B, S = (4, 512)
        EPS_ATTN = 1e-06
        EPS_LN = 1e-06

        def _ln(x, scale, bias):
            m = jnp.mean(x, axis=-1, keepdims=True)
            v = jnp.var(x, axis=-1, keepdims=True)
            return (x - m) * jax.lax.rsqrt(v + EPS_LN) * scale + bias

        def _forward(x, Wq, bq, Wk, bk, Wv, bv, Wo, bo, ln1_s, ln1_b, W1, b1, W2, b2, ln2_s, ln2_b):
            gelu = lambda t: jax.nn.gelu(t, approximate=True)
            fmap = lambda t: jax.nn.elu(t) + 1.0
            for i in range(NUM_BLOCKS):
                residual = x
                Q = fmap(x @ Wq[i] + bq[i])
                K = fmap(x @ Wk[i] + bk[i])
                value = x @ Wv[i] + bv[i]
                KV = jnp.einsum('nsh,nsh->nh', K, value)
                Ksum = jnp.sum(K, axis=1)
                Z = 1.0 / (Q * Ksum[:, None, :] + EPS_ATTN)
                V = Q * KV[:, None, :] * Z
                attn_out = gelu(V @ Wo[i] + bo[i])
                x = _ln(attn_out + residual, ln1_s[i], ln1_b[i])
                residual = x
                h = gelu(x @ W1[i] + b1[i])
                ff_out = gelu(h @ W2[i] + b2[i])
                x = _ln(ff_out + residual, ln2_s[i], ln2_b[i])
            return x
        return _forward(x, Wq, bq, Wk, bk, Wv, bv, Wo, bo, ln1_s, ln1_b, W1, b1, W2, b2, ln2_s, ln2_b)

    def _L1_ffn_ref(hidden_states, W, b, lora_down, lora_up, down_aux, up_aux):
        import jax, jax.numpy as jnp
        import numpy as np
        ALPHA = 1.0
        lilora_weight = up_aux @ (lora_up @ (lora_down @ down_aux))
        base = jnp.einsum('bsi,oi->bso', hidden_states, W) + b
        delta = jnp.einsum('bsi,oi->bso', hidden_states, lilora_weight)
        return base + ALPHA * delta
    x = L0_attn_x
    mod = (_silu(L0_c) @ L0_wmod).reshape(L0_c.shape[0], 6, 1, -1)
    sa, ca, ga, sb, cb, gb = (mod[:, 0], mod[:, 1], mod[:, 2], mod[:, 3], mod[:, 4], mod[:, 5])
    ga = (2 * (ga >= 0) - 1) * jnp.maximum(jnp.abs(ga), 0.25)
    gb = (2 * (gb >= 0) - 1) * jnp.maximum(jnp.abs(gb), 0.25)
    h = _layernorm(x, axis=-1) * (1 + ca) + sa
    x = x + ga * _L0_attn_ref(h, L0_attn_w_qkv, L0_attn_b_qkv, L0_attn_w_out, L0_attn_b_out)
    h = _layernorm(x, axis=-1) * (1 + cb) + sb
    x = x + gb * _L0_ffn_ref(h, L0_ffn_Wg, L0_ffn_W1, L0_ffn_W2, L0_ffn_W3)
    mod = (_silu(L1_c) @ L1_wmod).reshape(L1_c.shape[0], 6, 1, -1)
    sa, ca, ga, sb, cb, gb = (mod[:, 0], mod[:, 1], mod[:, 2], mod[:, 3], mod[:, 4], mod[:, 5])
    ga = (2 * (ga >= 0) - 1) * jnp.maximum(jnp.abs(ga), 0.25)
    gb = (2 * (gb >= 0) - 1) * jnp.maximum(jnp.abs(gb), 0.25)
    h = _layernorm(x, axis=-1) * (1 + ca) + sa
    x = x + ga * _L1_attn_ref(h, L1_attn_Wq, L1_attn_bq, L1_attn_Wk, L1_attn_bk, L1_attn_Wv, L1_attn_bv, L1_attn_Wo, L1_attn_bo, L1_attn_ln1_s, L1_attn_ln1_b, L1_attn_W1, L1_attn_b1, L1_attn_W2, L1_attn_b2, L1_attn_ln2_s, L1_attn_ln2_b)
    h = _layernorm(x, axis=-1) * (1 + cb) + sb
    x = x + gb * _L1_ffn_ref(h, L1_ffn_W, L1_ffn_b, L1_ffn_lora_down, L1_ffn_lora_up, L1_ffn_down_aux, L1_ffn_up_aux)
    return x

_drawn_inputs = setup_inputs


def setup_inputs(seed=0):
    import zlib

    import numpy as np

    out = dict(_drawn_inputs(seed))
    spreads = {'L1_attn_bq': (0.0, 2.0),
     'L1_attn_bk': (0.0, 2.0),
     'L1_attn_bv': (0.0, 0.1),
     'L1_attn_bo': (0.0, 0.1),
     'L1_attn_ln1_s': (1.0, 0.2),
     'L1_attn_ln1_b': (0.0, 0.1),
     'L1_attn_b1': (0.0, 0.323),
     'L1_attn_b2': (0.0, 0.1),
     'L1_attn_ln2_s': (1.0, 0.2),
     'L1_attn_ln2_b': (0.0, 0.1)}
    factors = {'L0_attn_b_qkv': 8.0,
     'L0_attn_b_out': 8.0,
     'L0_ffn_Wg': 8.0,
     'L0_ffn_W1': 8.0,
     'L0_ffn_W2': 8.0,
     'L0_ffn_W3': 8.0,
     'L1_attn_Wq': 22.237,
     'L1_ffn_b': 170.704,
     'L1_ffn_lora_down': 8.0,
     'L1_ffn_lora_up': 8.0,
     'L1_ffn_down_aux': 8.0,
     'L1_ffn_up_aux': 8.0,
     'L1_ffn_W': 8.0}
    for name, (base, spread) in spreads.items():
        noise = np.random.default_rng([zlib.crc32(name.encode()), seed]).standard_normal(out[name].shape)
        drawn = base * np.exp(spread * noise) if base else spread * noise
        out[name] = jnp.asarray(drawn.astype(out[name].dtype))
    for name, factor in factors.items():
        out[name] = (out[name] * factor).astype(out[name].dtype)
    return out
```

```python
from contextlib import ExitStack

import numpy as np
import concourse.bass as bass
from concourse import mybir

F32 = mybir.dt.float32
F32R = mybir.dt.float32r
BF16 = mybir.dt.bfloat16
ALU = mybir.AluOpType
ACT = mybir.ActivationFunctionType
AX = mybir.AxisListType

P = 128
B, S, D = 32, 256, 128
T = B * S
CH = 2 * S
NCH = T // CH
KT = CH // P
H, HD, WINDOW = 16, 8, 64
KEYS = P + WINDOW
E, HID = 8, 352
NHC = E * HID // P
BLOCKS, FF = 8, 512
LORA_D, LORA_R, LORA_U = 100, 4, 50
SCALE = HD ** -0.5
NSTACK = 16
EPS_LN, EPS_BLK, EPS_ATTN = 1e-5, 1e-6, 1e-6
WA_COLS = 3 * D + 3
WB_COLS = D + 2 * FF + 10


class Chip:
    pass


class LnBuffers:

    def __init__(self, sb, name):
        self.stats = sb(f"{name}_stats", [P, KT, 6])
        self.mv = sb(f"{name}_mv", [P, KT, 2])
        self.var = sb(f"{name}_var", [P, KT])
        self.rstd = sb(f"{name}_rstd", [P, KT])


def transpose_tiles(nc, out, src, ident):
    for k in range(KT):
        s = slice(k * P, (k + 1) * P)
        ins = nc.tensor.transpose(out[:, s], src[:, s], ident[:])
    return ins


def ln_stats(nc, dve, ln, ps, chain, n, var_ready, eps):
    for k in range(KT):
        ins = nc.vector.bn_stats(ln.stats[:, k, :], ps[:, k * P:(k + 1) * P])
    ins.then_inc(chain, 1)
    dve.wait_ge(chain, 3 * n + 1)
    dve.sem_inc(chain, 1)
    for k in range(KT):
        ins = nc.vector.bn_aggr(ln.mv[:, k, :], ln.stats[:, k, :])
    ins.then_inc(chain, 1)
    dve.wait_ge(chain, 3 * n + 3)
    nc.vector.tensor_scalar(ln.var[:], ln.mv[:, :, 1], eps, None, ALU.add).then_inc(var_ready, 1)


def ln_apply(nc, ln, z, ps):
    for k in range(KT):
        s = slice(k * P, (k + 1) * P)
        ins = nc.vector.tensor_scalar(z[:, s], ps[:, s], ln.mv[:, k, 0:1], ln.rstd[:, k:k + 1], ALU.subtract, ALU.mult)
    return ins


def modulate(nc, m, out, ps, layer, shift, chunk):
    for b in range(2):
        s = slice(b * S, (b + 1) * S)
        col = bass.ds(chunk * 2 + b, 1)
        ins = nc.scalar.activation(out[:, s], ps[:, s], ACT.Identity, bias=m.mod[:, layer, shift, col],
                                   scale=m.mod[:, layer, shift + 1, col])
    return ins


def run_setup(nc, m):
    d = m.dram
    with ExitStack() as ctx:
        sb = lambda name, shape, dt=F32: ctx.enter_context(nc.sbuf_tensor(name, shape, dt))
        sem = lambda name: ctx.enter_context(nc.semaphore(name))
        ps_mod = ctx.enter_context(nc.psum_tensor("ps_mod", [P, 2, 6, B], F32))
        ps_lora = ctx.enter_context(nc.psum_tensor("ps_lora", [P, 3, P], F32))
        cond, cond_silu = sb("cond", [P, 2, B]), sb("cond_silu", [P, 2, B])
        wmod = sb("wmod", [P, 2, 6 * D])
        down_t, down_aux = sb("down_t", [LORA_D, LORA_R]), sb("down_aux", [LORA_D, D])
        up_t, up_aux_t = sb("up_t", [LORA_R, LORA_U]), sb("up_aux_t", [LORA_U, D])
        low, mid = sb("low", [LORA_R, D]), sb("mid", [LORA_U, D])
        w_t = sb("w_t", [P, D])
        sign, size = sb("sign", [P, 2, 2, B]), sb("size", [P, 2, 2, B])
        misc = sb("misc", [P, 5 + D + E])
        masks_f, stack_f = sb("masks_f", [P, 2 * KEYS]), sb("stack_f", [P, NSTACK, P])
        mod_loaded, lora_loaded, const_loaded, resident = (sem(k) for k in ("mod_loaded", "lora_loaded", "const_loaded", "resident"))
        silu_done, mod_done, low_ready, low_sb, mid_ready, mid_sb, lora_ready, dve_step = (sem(k) for k in (
            "silu_done", "mod_done", "low_ready", "low_sb", "mid_ready", "mid_sb", "lora_ready", "dve_step"))
        block = ctx.enter_context(nc.Block())

        @block.sync
        def _(sp):
            sp.dma_start(cond[:], d["cond"]).then_inc(mod_loaded, 16)
            sp.dma_start(wmod[:], d["wmod"]).then_inc(mod_loaded, 16)
            for dst, src in ((down_t, d["down_t"]), (down_aux, d["down_aux"]), (up_t, d["up_t"]), (up_aux_t, d["up_aux_t"]), (w_t, d["w_t"])):
                sp.dma_start(dst[:], src).then_inc(lora_loaded, 16)
            sp.dma_start(stack_f[:], d["stack"]).then_inc(const_loaded, 16)
            sp.dma_start(masks_f[:], d["masks"]).then_inc(const_loaded, 16)
            sp.dma_start(misc[:], d["misc"]).then_inc(const_loaded, 16)
            sp.dma_start(m.ident[:], d["ident"]).then_inc(resident, 16)
            sp.dma_start(m.w_qkv[:], d["w_qkv"]).then_inc(resident, 16)
            sp.dma_start(m.w_out[:], d["w_out"]).then_inc(resident, 16)
            sp.dma_start(m.w_gate[:], d["w_gate"]).then_inc(resident, 16)
            sp.wait_ge(resident, 4 * 16)

        @block.scalar
        def _(act):
            act.wait_ge(mod_loaded, 32)
            nc.scalar.activation(cond_silu[:], cond[:], ACT.Silu).then_inc(silu_done, 1)

        @block.tensor
        def _(pe):
            pe.wait_ge(silu_done, 1)
            for layer in range(2):
                for k in range(6):
                    mm = nc.tensor.matmul(ps_mod[:, layer, k, :], wmod[:, layer, k * D:(k + 1) * D], cond_silu[:, layer, :],
                                          start=True, stop=True)
            mm.then_inc(mod_done, 1)
            pe.wait_ge(lora_loaded, 5 * 16)
            nc.tensor.matmul(ps_lora[0:LORA_R, 0, :], down_t[:], down_aux[:], start=True, stop=True).then_inc(low_ready, 1)
            pe.wait_ge(low_sb, 1)
            nc.tensor.matmul(ps_lora[0:LORA_U, 1, :], up_t[:], low[:], start=True, stop=True).then_inc(mid_ready, 1)
            pe.wait_ge(mid_sb, 1)
            nc.tensor.matmul(ps_lora[:, 2, :], mid[:], up_aux_t[:], start=True, stop=True).then_inc(lora_ready, 1)

        @block.vector
        def _(dve):
            nc.vector.memset(m.neg_half[:], -0.5)
            nc.vector.memset(m.m_cols[:], 0.0)
            nc.vector.memset(m.ones_v[:], 1.0)
            nc.vector.memset(m.v_aug[:], 0.0).then_inc(dve_step, 1)
            dve.wait_ge(mod_done, 1)
            nc.vector.tensor_copy(m.mod[:], ps_mod[:]).then_inc(dve_step, 1)
            dve.wait_ge(dve_step, 2)
            by3 = m.mod[:].rearrange("p l (a k) b -> p l a k b", k=3)
            scale, gain = by3[:, :, :, 1, :], by3[:, :, :, 2, :]
            nc.vector.tensor_scalar(scale, scale, 1.0, None, ALU.add)
            nc.vector.tensor_scalar(sign[:], gain, 0.0, 2.0, ALU.is_ge, ALU.mult).then_inc(dve_step, 1)
            dve.wait_ge(dve_step, 3)
            nc.vector.tensor_scalar(sign[:], sign[:], -1.0, None, ALU.add).then_inc(dve_step, 1)
            dve.wait_ge(dve_step, 4)
            nc.vector.tensor_tensor(size[:], sign[:], gain, ALU.mult).then_inc(dve_step, 1)
            dve.wait_ge(dve_step, 5)
            nc.vector.tensor_scalar(size[:], size[:], 0.25, None, ALU.max).then_inc(dve_step, 1)
            dve.wait_ge(dve_step, 6)
            nc.vector.tensor_tensor(gain, sign[:], size[:], ALU.mult).then_inc(dve_step, 1)
            dve.wait_ge(const_loaded, 48)
            nc.vector.tensor_copy(m.stack[:], stack_f[:])
            nc.vector.tensor_copy(m.masks[:], masks_f[:])
            nc.vector.tensor_copy(m.misc[:], misc[:])
            nc.vector.tensor_scalar(m.bq_scaled[:], misc[:, 0:1], SCALE, None, ALU.mult)
            dve.wait_ge(resident, 4 * 16)
            nc.vector.tensor_copy(m.ident_b[:], m.ident[:])
            dve.wait_ge(dve_step, 7)
            nc.vector.tensor_scalar(m.gain_bout[:], m.mod[:, 0, 2, :], misc[:, 2:3], None, ALU.mult)
            nc.vector.tensor_scalar(m.gain_bffn[:], m.mod[:, 1, 5, :], misc[:, 3:4], None, ALU.mult)
            dve.wait_ge(low_ready, 1)
            nc.vector.tensor_copy(low[:], ps_lora[0:LORA_R, 0, :]).then_inc(low_sb, 1)
            dve.wait_ge(mid_ready, 1)
            nc.vector.tensor_copy(mid[:], ps_lora[0:LORA_U, 1, :]).then_inc(mid_sb, 1)
            dve.wait_ge(lora_ready, 1)
            nc.vector.tensor_tensor(m.w_ffn[:], ps_lora[:, 2, :], w_t[:], ALU.add).then_inc(dve_step, 1)
            dve.wait_ge(dve_step, 8)


EXPERTS_IN, BLOCKS_IN, LAST = range(3)


def run_norm_phase(nc, m, mode):
    layer, shift = ((0, 3), (1, 0), (1, 3))[mode]
    with ExitStack() as ctx:
        sb = lambda name, shape, dt=F32: ctx.enter_context(nc.sbuf_tensor(f"n{mode}_{name}", shape, dt))
        sem = lambda name: ctx.enter_context(nc.semaphore(f"n{mode}_{name}"))
        banks = [ctx.enter_context(nc.psum_tensor(f"n{mode}_bank{k}", [P, CH], F32)) for k in range(6)]
        ps_x, ps_z, ps_out = banks[0:2], banks[2:4], banks[4:6]
        x_in, z, h, y, out = (sb(k, [P, 2, CH]) for k in ("x_in", "z", "h", "y", "out"))
        ln = [LnBuffers(sb, f"ln{p}") for p in range(2)]
        x_ready, x_kept, pe_xt, var, rstd, dve_z, pe_zt, act_h, pe_out, dve_h, act_y, dve_out, chain, stored = (sem(k) for k in (
            "x_ready", "x_kept", "pe_xt", "var", "rstd", "dve_z", "pe_zt", "act_h", "pe_out", "dve_h", "act_y", "dve_out",
            "chain", "stored"))
        follows = mode != BLOCKS_IN
        block = ctx.enter_context(nc.Block())

        def turns(eng, turn):
            turn(0, 0, mid=False, last=False)
            turn(1, 1, last=False)
            with eng.Fori(2, NCH - 1, 2) as i:
                turn(i, 0)
                turn(i + 1, 1)
            turn(NCH, 0, first=False)
            if follows:
                turn(NCH + 1, 1, first=False, mid=False)

        if mode == EXPERTS_IN:
            @block.sync
            def _(sp):
                for k, src in enumerate((m.dram["w1"], m.dram["w3"])):
                    sp.dma_start(m.staged[:, k, :], src).then_inc(stored, 16)
                sp.wait_ge(stored, 32)

        if mode == LAST:
            @block.sync
            def _(sp):
                def store(i, p):
                    sp.wait_ge(dve_out, i + 1)
                    sp.dma_start(m.out[:, bass.ds(i * CH, CH)], out[:, p, :]).then_inc(stored, 16)

                with sp.Fori(0, NCH - 1, 2) as i:
                    store(i, 0)
                    store(i + 1, 1)
                sp.wait_ge(stored, NCH * 16)

        @block.gpsimd
        def _(pool):
            def source(i, p, wait=True):
                s = bass.ds(i * CH, CH)
                if mode == LAST:
                    pool.wait_ge(x_ready, i + 1)
                    nc.gpsimd.tensor_copy(m.X[:, s], x_in[:, p, :]).then_inc(x_kept, 1)
                else:
                    if wait:
                        pool.wait_ge(pe_xt, i - 1)
                    nc.gpsimd.tensor_copy(x_in[:, p, :], m.X[:, s]).then_inc(x_ready, 1)

            def power(i, p):
                pool.wait_ge(var, i + 1)
                nc.gpsimd.tensor_tensor(ln[p].rstd[:], ln[p].var[:], m.neg_half[:], ALU.pow).then_inc(rstd, 1)

            if mode == LAST:
                with pool.Fori(0, NCH - 1, 2) as i:
                    for k in range(2):
                        source(i + k, k)
                        power(i + k, k)
            else:
                source(0, 0, False)
                source(1, 1, False)
                with pool.Fori(0, NCH - 3, 2) as i:
                    for k in range(2):
                        power(i + k, k)
                        source(i + k + 2, k)
                power(NCH - 2, 0)
                power(NCH - 1, 1)

        @block.tensor
        def _(pe):
            def turn(i, p, first=True, mid=True, last=True):
                if first:
                    pe.wait_ge(x_ready, i + 1)
                    if mid and last:
                        pe.wait_ge(dve_z, i - 1)
                    transpose_tiles(nc, ps_x[p], x_in[:, p, :], m.ident).then_inc(pe_xt, 1)
                if mid:
                    pe.wait_ge(dve_z, i)
                    if last:
                        pe.wait_ge(act_h, i - 2)
                    transpose_tiles(nc, ps_z[1 - p], z[:, 1 - p, :], m.ident).then_inc(pe_zt, 1)
                if last and mode == EXPERTS_IN:
                    pe.wait_ge(act_h, i - 1)
                    for k in range(KT):
                        mm = nc.tensor.matmul(ps_out[0][:, bass.ds((i - 2) * KT * E + k * E, E)], h[:, p, k * P:(k + 1) * P],
                                              m.w_gate[:], start=True, stop=True)
                    mm.then_inc(pe_out, 1)
                if last and mode == LAST:
                    pe.wait_ge(act_h, i - 1)
                    pe.wait_ge(act_y, i - 2)
                    nc.tensor.matmul(ps_out[p][:], m.w_ffn[:], h[:, p, :], start=True, stop=True).then_inc(pe_out, 1)

            turns(pe, turn)

        @block.scalar
        def _(act):
            def turn(i, p, first=True, mid=True, last=True):
                if mid:
                    act.wait_ge(pe_zt, i)
                    if last and mode == EXPERTS_IN:
                        act.wait_ge(pe_out, i - 2)
                        act.wait_ge(dve_h, i - 2)
                    dst = m.XB[:, bass.ds((i - 1) * CH, CH)] if mode == BLOCKS_IN else h[:, 1 - p, :]
                    modulate(nc, m, dst, ps_z[1 - p], layer, shift, i - 1).then_inc(act_h, 1)
                if last and mode == LAST:
                    act.wait_ge(pe_out, i - 1)
                    act.wait_ge(dve_out, i - 2)
                    for b in range(2):
                        s, col = slice(b * S, (b + 1) * S), bass.ds((i - 2) * 2 + b, 1)
                        ins = nc.scalar.activation(y[:, p, s], ps_out[p][:, s], ACT.Identity, bias=m.gain_bffn[:, col],
                                                   scale=m.mod[:, 1, 5, col])
                    ins.then_inc(act_y, 1)

            turns(act, turn)

        @block.vector
        def _(dve):
            def turn(i, p, first=True, mid=True, last=True):
                if first:
                    if mode == LAST:
                        if last:
                            dve.wait_ge(x_kept, i - 1)
                        for b in range(2):
                            s = bass.ds(i * CH + b * S, S)
                            ins = nc.vector.scalar_tensor_tensor(x_in[:, p, b * S:(b + 1) * S], m.XB[:, s],
                                                                 m.mod[:, 1, 2, bass.ds(i * 2 + b, 1)], m.X[:, s], ALU.mult, ALU.add)
                        ins.then_inc(x_ready, 1)
                    dve.wait_ge(pe_xt, i + 1)
                    ln_stats(nc, dve, ln[p], ps_x[p], chain, i, var, EPS_LN)
                if last and mode == EXPERTS_IN:
                    dve.wait_ge(act_h, i - 1)
                    nc.vector.tensor_copy(m.XB[:, bass.ds((i - 2) * CH, CH)], h[:, p, :]).then_inc(dve_h, 1)
                if last and mode == LAST:
                    dve.wait_ge(act_y, i - 1)
                    dve.wait_ge(x_kept, i - 1)
                    dve.wait_ge(stored, (i - 2) * 16)
                    nc.vector.tensor_tensor(out[:, p, :], y[:, p, :], m.X[:, bass.ds((i - 2) * CH, CH)], ALU.add).then_inc(dve_out, 1)
                if first:
                    dve.wait_ge(rstd, i + 1)
                    ln_apply(nc, ln[p], z[:, p, :], ps_x[p]).then_inc(dve_z, 1)

            turns(dve, turn)
            if mode == EXPERTS_IN:
                dve.wait_ge(pe_out, NCH)
                nc.vector.tensor_copy(m.logits[:], ps_out[0][:]).then_inc(dve_out, 1)


def run_attention_inputs(nc, m):
    with ExitStack() as ctx:
        sb = lambda name, shape, dt=F32: ctx.enter_context(nc.sbuf_tensor(name, shape, dt))
        sem = lambda name: ctx.enter_context(nc.semaphore(name))
        banks = [ctx.enter_context(nc.psum_tensor(f"in_bank{k}", [P, CH], F32)) for k in range(8)]
        ps_x, ps_z, ps_q, ps_k, ps_v = banks[0:2], banks[2], banks[3:5], banks[5:7], banks[7]
        x_in, z, h = sb("x_in", [P, 2, CH]), sb("z", [P, 2, CH]), sb("h_in", [P, 2, CH])
        ln = [LnBuffers(sb, f"in{p}") for p in range(2)]
        x_loaded = [sem("x_loaded0"), sem("x_loaded1")]
        pe_xt, var, rstd, dve_z, pe_zt, act_h, pe_q, act_q, pe_v, dve_v, chain, kept = (sem("in_" + k) for k in (
            "pe_xt", "var", "rstd", "dve_z", "pe_zt", "act_h", "pe_q", "act_q", "pe_v", "dve_v", "chain", "kept"))
        block = ctx.enter_context(nc.Block())
        x_dram = m.dram["x"]

        @block.sync
        def _(sp):
            def load(i, p):
                sp.wait_ge(pe_xt, i)
                s = bass.ds(i * CH, CH)
                sp.dma_start(x_in[:, p, :], x_dram[:, s]).then_inc(x_loaded[p], 16)
                sp.dma_start(m.X[:, s], x_dram[:, s]).then_inc(kept, 16)

            with sp.Fori(0, NCH - 1, 2) as i:
                load(i, 0)
                load(i + 1, 1)
            sp.wait_ge(kept, NCH * 16)

        @block.tensor
        def _(pe):
            pe.sem_inc(pe_xt, 1)

            def turn(i, p, half, first=True, mid=True, last=True):
                if first:
                    pe.wait_ge(x_loaded[p], half * 16 + 16)
                    if mid:
                        pe.wait_ge(dve_z, i - 1)
                    transpose_tiles(nc, ps_x[p], x_in[:, p, :], m.ident).then_inc(pe_xt, 1)
                if mid:
                    pe.wait_ge(dve_z, i)
                    pe.wait_ge(act_h, i - 1)
                    transpose_tiles(nc, ps_z, z[:, 1 - p, :], m.ident).then_inc(pe_zt, 1)
                if last:
                    pe.wait_ge(act_h, i - 1)
                    pe.wait_ge(act_q, i - 2)
                    nc.tensor.matmul(ps_q[p][:], m.w_qkv[:, 0:D], h[:, p, :], start=True, stop=True)
                    nc.tensor.matmul(ps_k[p][:], m.w_qkv[:, D:2 * D], h[:, p, :], start=True, stop=True).then_inc(pe_q, 1)
                    pe.wait_ge(dve_v, i - 2)
                    for k in range(KT):
                        s = slice(k * P, (k + 1) * P)
                        mm = nc.tensor.matmul(ps_v[:, s], h[:, p, s], m.w_qkv[:, 2 * D:3 * D], start=True, stop=True)
                    mm.then_inc(pe_v, 1)

            turn(0, 0, 0, mid=False, last=False)
            turn(1, 1, 0, last=False)
            with pe.Fori(1, NCH // 2) as k:
                turn(2 * k, 0, k)
                turn(2 * k + 1, 1, k)
            turn(NCH, 0, 0, first=False)
            turn(NCH + 1, 1, 0, first=False, mid=False)

        @block.gpsimd
        def _(pool):
            def power(i, p):
                pool.wait_ge(var, i + 1)
                nc.gpsimd.tensor_tensor(ln[p].rstd[:], ln[p].var[:], m.neg_half[:], ALU.pow).then_inc(rstd, 1)

            with pool.Fori(0, NCH - 1, 2) as i:
                power(i, 0)
                power(i + 1, 1)

        @block.scalar
        def _(act):
            def turn(i, p, mid=True, last=True):
                if mid:
                    act.wait_ge(pe_zt, i)
                    ins = modulate(nc, m, h[:, 1 - p, :], ps_z, 0, 0, i - 1)
                    ins.then_inc(act_h, 1)
                if last:
                    act.wait_ge(pe_q, i - 1)
                    s = bass.ds((i - 2) * CH, CH)
                    nc.scalar.activation(m.XB[:, s], ps_q[p][:], ACT.Identity, bias=m.bq_scaled[:], scale=SCALE)
                    nc.scalar.activation(m.k_all[:, s], ps_k[p][:], ACT.Identity, bias=m.misc[:, 1:2]).then_inc(act_q, 1)

            turn(1, 1, last=False)
            with act.Fori(2, NCH - 1, 2) as i:
                turn(i, 0)
                turn(i + 1, 1)
            turn(NCH, 0)
            turn(NCH + 1, 1, mid=False)

        @block.vector
        def _(dve):
            def turn(i, p, first=True, last=True):
                if first:
                    dve.wait_ge(pe_xt, i + 2)
                    ln_stats(nc, dve, ln[p], ps_x[p], chain, i, var, EPS_LN)
                if last:
                    dve.wait_ge(pe_v, i - 1)
                    bias = m.misc[:, 5:5 + D].unsqueeze(1).broadcast_to([P, KT, D])
                    nc.vector.tensor_tensor(m.v_all[:, bass.ds((i - 2) * CH, CH)].rearrange("p (k d) -> p k d", k=KT),
                                            ps_v[:].rearrange("p (k d) -> p k d", k=KT), bias, ALU.add).then_inc(dve_v, 1)
                if first:
                    dve.wait_ge(rstd, i + 1)
                    ln_apply(nc, ln[p], z[:, p, :], ps_x[p]).then_inc(dve_z, 1)

            turn(0, 0, last=False)
            turn(1, 1, last=False)
            with dve.Fori(2, NCH - 1, 2) as i:
                turn(i, 0)
                turn(i + 1, 1)
            turn(NCH, 0, first=False)
            turn(NCH + 1, 1, first=False)


def run_attention(nc, m):
    R = H // 2
    with ExitStack() as ctx:
        sb = lambda name, shape, dt=F32: ctx.enter_context(nc.sbuf_tensor(name, shape, dt))
        sem = lambda name: ctx.enter_context(nc.semaphore("at_" + name))
        psum = lambda name, shape: ctx.enter_context(nc.psum_tensor(name, shape, F32))
        ps_qs, ps_ks = psum("ps_qs", [P, 2, CH]), psum("ps_ks", [P, 2, CH])
        ps_pv, ps_s, ps_t = psum("ps_pv", [P, 2, CH]), psum("ps_s", [P, 2, S]), psum("ps_t", [P, CH])
        high, low = sb("part_high", [P, 2, S], F32R), sb("part_low", [P, 2, S], F32R)
        q_st, k_st = sb("q_st", [P, 2, 4, S], F32R), sb("k_st", [P, 2, 4, S], F32R)
        probs = sb("probs", [P, 2, 2, 2 * KEYS])
        mx, mx_high = sb("mx", [P, 2, 4, 2]), sb("mx_high", [P, 2, 4, 2], F32R)
        den_ln, den_inv, att_t, out_t = sb("den_ln", [P, S]), sb("den_inv", [P, S]), sb("att_t", [P, 2, 4, S]), sb("out_t", [P, S])
        pe_qs, pe_ks, pe_pv, pe_sel, pe_mt, pe_op = (sem(k) for k in ("pe_qs", "pe_ks", "pe_pv", "pe_sel", "pe_mt", "pe_op"))
        dve_mx, dve_mh, dve_m, dve_q2, dve_high, dve_hl, dve_on, dve_x = (sem(k) for k in (
            "dve_mx", "dve_mh", "dve_m", "dve_q2", "dve_high", "dve_hl", "dve_on", "dve_x"))
        act_st, act_p, act_ln, act_inv, act_op, pool_v = (sem(k) for k in ("act_st", "act_p", "act_ln", "act_inv", "act_op", "pool_v"))
        block = ctx.enter_context(nc.Block())

        def places(r):
            low, high = slice(0, P // 2), slice(P // 2, P)
            return (low, high) if r % 2 == 0 else (high, low)

        def turns(eng, turn):
            turn(0, 0, k=False, o=False)
            turn(1, 1, o=False)
            with eng.Fori(2, B - 3, 2) as i:
                turn(i, 0)
                turn(i + 1, 1)
            turn(B - 2, 0)
            turn(B - 1, 1, s=False)
            turn(B, 0, q=False, s=False)
            turn(B + 1, 1, q=False, k=False, s=False)

        @block.tensor
        def _(pe):
            pe.sem_inc(pe_pv, 1)

            def q_round(i, p, r):
                if r % 2 == 0:
                    pe.wait_ge(act_st, 8 * i + r + 2)
                pe.wait_ge(dve_mx, R * i + r)
                g = r // 2
                for jj in range(2):
                    rows = slice(32 * (2 * (r % 2) + jj), 32 * (2 * (r % 2) + jj) + 32)
                    for t in range(2):
                        nc.tensor.matmul(ps_qs[:, jj, t * KEYS:(t + 1) * KEYS], q_st[rows, p, g, t * P:(t + 1) * P],
                                         k_st[rows, p, g, t * WINDOW:t * WINDOW + KEYS], start=(t == 0), stop=False,
                                         skip_group_check=True)
                    mm = nc.tensor.matmul(ps_qs[:, jj, 0:2 * KEYS], m.ident_b[:], m.masks[:], start=False, stop=True,
                                          skip_group_check=True)
                mm.then_inc(pe_qs, 1)

            def k_round(i, p, r):
                g = r // 2
                if r % 2 == 0:
                    pe.wait_ge(dve_q2, 4 * i + g + 1)
                pe.wait_ge(act_p, R * i + r)
                for jj in range(2):
                    rows = slice(32 * (2 * (r % 2) + jj), 32 * (2 * (r % 2) + jj) + 32)
                    for t in range(2):
                        nc.tensor.matmul(ps_ks[:, jj, t * KEYS:(t + 1) * KEYS], k_st[rows, p, g, t * P:(t + 1) * P],
                                         q_st[rows, p, g, t * WINDOW:t * WINDOW + KEYS], start=(t == 0), stop=False,
                                         skip_group_check=True)
                    mm = nc.tensor.matmul(ps_ks[:, jj, 0:2 * KEYS], m.ident_b[:], m.masks[:], start=False, stop=True,
                                          skip_group_check=True)
                mm.then_inc(pe_ks, 1)

            def pv_round(i, p, r):
                pe.wait_ge(act_p, R * i + r + 1)
                if r == 0:
                    pe.wait_ge(pool_v, i + 1)
                pe.wait_ge(dve_on, R * i + r + 1)
                v_rows, sum_rows = places(r)
                for t in range(2):
                    cols = slice(t * WINDOW, t * WINDOW + KEYS)
                    for jj in range(2):
                        pr = probs[:, r % 2, jj, t * KEYS:(t + 1) * KEYS]
                        v, s = v_rows.start + 32 * jj, sum_rows.start + 32 * jj
                        nc.tensor.matmul(ps_pv[v:v + 32, r % 2, cols], m.v_aug[:, p, t, 2 * r + jj, :], pr,
                                         start=(t == 0), stop=(t == 1), skip_group_check=True)
                        mm = nc.tensor.matmul(ps_pv[s:s + 32, r % 2, cols], m.ones_v[:], pr,
                                              start=(t == 0), stop=(t == 1), skip_group_check=True)
                mm.then_inc(pe_pv, 1)

            def select(i, g):
                if g == 0:
                    pe.wait_ge(dve_hl, i + 1)
                if g or not isinstance(i, int) or i:
                    pe.wait_ge(act_st, 8 * i + 2 * g)
                for which in range(2):
                    for part, src in enumerate((high, low)):
                        mm = nc.tensor.matmul(ps_s[:, which, :], m.stack[:, (2 * which + part) * 4 + g, :], src[:, which, :],
                                              start=(part == 0), stop=(part == 1))
                mm.then_inc(pe_sel, 1)

            def max_rows(i, g):
                pe.wait_ge(dve_m, 4 * i + g + 1)
                for t in range(2):
                    mm = nc.tensor.transpose(ps_t[:, t * P:(t + 1) * P], m.m_cols[:, g % 2, t, :], m.ident[:])
                mm.then_inc(pe_mt, 1)

            def turn(i, p, q=True, k=True, o=True, s=True):
                for r in range(R):
                    if q:
                        q_round(i, p, r)
                    if k:
                        k_round(i - 1, 1 - p, r)
                    if r and k:
                        pv_round(i - 1, 1 - p, r - 1)
                    if r == 0 and o:
                        pv_round(i - 2, p, R - 1)
                    if r == 0 and q and k:
                        select(i, 3)
                    if r == 1 and k:
                        pe.wait_ge(dve_q2, 4 * i - 1)
                        max_rows(i - 1, 3)
                    if r in (2, 4, 6) and s:
                        select(i + 1, r // 2 - 1)
                    if r == 2 and q:
                        if k:
                            pe.wait_ge(dve_q2, 4 * i)
                        max_rows(i, 0)
                    if r == 3 and o:
                        pe.wait_ge(dve_on, R * (i - 1) + 2)
                        if q:
                            pe.wait_ge(dve_q2, 4 * i + 1)
                        elif k:
                            pe.wait_ge(dve_q2, 4 * i)
                        for g in range(4):
                            mm = nc.tensor.matmul(ps_t[:, 0:S], m.w_out[:, g, :], att_t[:, p, g, :], start=(g == 0), stop=(g == 3))
                        mm.then_inc(pe_op, 1)
                    if r == 4 and q:
                        if o:
                            pe.wait_ge(act_op, i - 1)
                        else:
                            pe.wait_ge(dve_q2, 4 * i + 1)
                        max_rows(i, 1)
                    if r == 6 and q:
                        pe.wait_ge(dve_q2, 4 * i + 2)
                        max_rows(i, 2)

            for g in range(4):
                select(0, g)
            turns(pe, turn)

        @block.scalar
        def _(act):
            def stack(i, p, g, k):
                act.wait_ge(pe_sel, 4 * i + g + 1)
                if k:
                    act.wait_ge(pe_ks, R * (i - 2) + 2 * g + 2)
                nc.scalar.activation(q_st[:, p, g, :], ps_s[:, 0, :], ACT.Copy).then_inc(act_st, 1)
                nc.scalar.activation(k_st[:, p, g, :], ps_s[:, 1, :], ACT.Identity, bias=m.misc[:, 4:5]).then_inc(act_st, 1)

            def inverse(i, r):
                n = R * i + r
                v_rows, sum_rows = places(r)
                act.wait_ge(pe_pv, n + 2)
                nc.scalar.activation(den_ln[v_rows, :], ps_pv[sum_rows, r % 2, 0:S], ACT.Ln).then_inc(act_ln, 1)
                act.wait_ge(act_ln, n + 1)
                nc.scalar.activation(den_inv[v_rows, :], den_ln[v_rows, :], ACT.Exp, scale=-1.0).then_inc(act_inv, 1)

            def turn(i, p, q=True, k=True, o=True, s=True):
                for r in range(R):
                    if k:
                        act.wait_ge(pe_ks, R * (i - 1) + r + 1)
                        act.wait_ge(pe_pv, R * (i - 1) + r)
                        nc.scalar.activation(probs[:, r % 2, :, :], ps_ks[:, :, 0:2 * KEYS], ACT.Exp).then_inc(act_p, 1)
                    if r and k:
                        inverse(i - 1, r - 1)
                    if r == 0 and o:
                        inverse(i - 2, R - 1)
                    if r == 4 and o:
                        act.wait_ge(pe_op, i - 1)
                        act.wait_ge(dve_x, i - 2)
                        col = bass.ds(i - 2, 1)
                        nc.scalar.activation(out_t[:], ps_t[:, 0:S], ACT.Identity, bias=m.gain_bout[:, col],
                                             scale=m.mod[:, 0, 2, col]).then_inc(act_op, 1)
                    if r == 1 and q and k:
                        stack(i, p, 3, o)
                    if r in (3, 5, 7) and s:
                        stack(i + 1, 1 - p, r // 2 - 1, k)

            nc.scalar.preload_act_table_set("natural_log_exp_and_others")
            for g in range(4):
                stack(0, 0, g, False)
            turns(act, turn)

        @block.gpsimd
        def _(pool):
            def v_copy(b, p):
                src = m.v_all[:, bass.ds(b * S, S)].rearrange("p (t h d) -> p t h d", t=2, h=H)
                nc.gpsimd.tensor_copy(m.v_aug[:, p, :, :, 0:HD], src).then_inc(pool_v, 1)

            v_copy(0, 0)
            v_copy(1, 1)
            with pool.Fori(2, B - 1, 2) as b:
                for k in range(2):
                    pool.wait_ge(pe_pv, R * (b + k) - R + 1)
                    v_copy(b + k, k)

        @block.vector
        def _(dve):
            def parts(i):
                if not isinstance(i, int) or i:
                    dve.wait_ge(pe_sel, 4 * i)
                for which, src in enumerate((m.XB, m.k_all)):
                    ins = nc.vector.tensor_copy(high[:, which, :], src[:, bass.ds(i * S, S)])
                ins.then_inc(dve_high, 1)
                dve.wait_ge(dve_high, i + 1)
                for which, src in enumerate((m.XB, m.k_all)):
                    ins = nc.vector.tensor_tensor(low[:, which, :], src[:, bass.ds(i * S, S)], high[:, which, :].bitcast(F32), ALU.subtract)
                ins.then_inc(dve_hl, 1)

            def maximum(i, r):
                dve.wait_ge(pe_qs, R * i + r + 1)
                g, odd = r // 2, r % 2
                nc.vector.tensor_reduce(mx[:, g % 2, 2 * odd:2 * odd + 2, :],
                                        ps_qs[:, :, 0:2 * KEYS].rearrange("p j (t c) -> p j t c", t=2), AX.X, ALU.max).then_inc(dve_mx, 1)
                if odd:
                    dve.wait_ge(dve_mx, R * i + r + 1)
                    nc.vector.tensor_scalar(mx_high[:, g % 2], mx[:, g % 2], -1.0, None, ALU.mult).then_inc(dve_mh, 1)
                    dve.wait_ge(dve_mh, 4 * i + g + 1)
                    cols = m.m_cols[:, g % 2].rearrange("p t (j c) -> p j t c", j=4)
                    nc.vector.tensor_copy(cols[:, :, :, 24], mx_high[:, g % 2].bitcast(F32))
                    nc.vector.scalar_tensor_tensor(cols[:, :, :, 25], mx[:, g % 2], -1.0, mx_high[:, g % 2].bitcast(F32),
                                                   ALU.mult, ALU.subtract).then_inc(dve_m, 1)

            def add_max(i, p, g):
                dve.wait_ge(pe_mt, 4 * i + g + 1)
                nc.vector.tensor_tensor(q_st[:, p, g, :], q_st[:, p, g, :].bitcast(F32), ps_t[:, 0:S], ALU.add).then_inc(dve_q2, 1)

            def normalise(i, p, r):
                rows = places(r)[0]
                dve.wait_ge(act_inv, R * i + r + 1)
                nc.vector.tensor_tensor(att_t[rows, p, r // 2, :], ps_pv[rows, r % 2, 0:S], den_inv[rows, :],
                                        ALU.mult).then_inc(dve_on, 1)

            def turn(i, p, q=True, k=True, o=True, s=True):
                for r in range(R):
                    if r == 2 and k:
                        add_max(i - 1, 1 - p, 3)
                    if q:
                        if r in (3, 5, 7):
                            add_max(i, p, r // 2 - 1)
                        maximum(i, r)
                    if k and r:
                        normalise(i - 1, 1 - p, r - 1)
                    if r == 0 and o:
                        normalise(i - 2, p, R - 1)
                    if r == 1 and s:
                        parts(i + 1)
                    if r == 5 and o:
                        dve.wait_ge(act_op, i - 1)
                        x = m.X[:, bass.ds((i - 2) * S, S)]
                        nc.vector.tensor_tensor(x, x, out_t[:], ALU.add).then_inc(dve_x, 1)

            dve.sem_inc(dve_on, 2)
            parts(0)
            turns(dve, turn)


def run_gate(nc, m):
    NT = T // P
    with ExitStack() as ctx:
        sb = lambda name, shape, dt=F32: ctx.enter_context(nc.sbuf_tensor("gate_" + name, shape, dt))
        sem = lambda name: ctx.enter_context(nc.semaphore("gate_" + name))
        ps_t = [ctx.enter_context(nc.psum_tensor(f"gate_ps{k}", [P, CH], F32)) for k in range(2)]
        logits, work, key, first, second, prob = (sb(k, [P, NT, E]) for k in ("logits", "work", "key", "first", "second", "prob"))
        red, inv = sb("red", [P, NT]), sb("inv", [P, NT])
        high = sb("high", [P, NT, E], F32R)
        parts = sb("parts", [P, NCH // 2, KT, 2, 32])
        step, exp_in, exp_out, ready, pe_t, act_t, act_high, act_pick, pool_low, w2_loaded, pick_loaded = (sem(k) for k in (
            "step", "exp_in", "exp_out", "ready", "pe_t", "act_t", "act_high", "act_pick", "pool_low", "w2_loaded", "pick_loaded"))
        block = ctx.enter_context(nc.Block())
        over = lambda v: v[:].unsqueeze(2).broadcast_to([P, NT, E])
        rank = m.misc[:, 5 + D:5 + D + E].unsqueeze(1).broadcast_to([P, NT, E])

        pairs = prob[:].rearrange("p (c q k) e -> p c q k e", q=2, k=KT)
        pairs_high = high[:].bitcast(F32).rearrange("p (c q k) e -> p c q k e", q=2, k=KT)

        @block.sync
        def _(sp):
            sp.wait_ge(pool_low, 1)
            sp.dma_start(m.staged[:, 0, :], m.dram["w2"]).then_inc(w2_loaded, 16)
            sp.wait_ge(pool_low, 2)
            sp.dma_start(m.staged[0:64, 1, :], m.dram["experts"]).then_inc(pick_loaded, 16)

        @block.gpsimd
        def _(pool):
            for k in range(3):
                pool.wait_ge(act_high, k + 1)
                nc.gpsimd.tensor_tensor(m.low[:, k, :], m.staged[:, k % 2, :], m.high[:, k, :].bitcast(F32),
                                        ALU.subtract).then_inc(pool_low, 1)

        @block.scalar
        def _(act):
            for k in range(2):
                nc.scalar.activation(m.high[:, k, :], m.staged[:, k, :], ACT.Copy).then_inc(act_high, 1)
            act.wait_ge(exp_in, 1)
            nc.scalar.activation(prob[:], work[:], ACT.Exp).then_inc(exp_out, 1)
            act.wait_ge(w2_loaded, 16)
            nc.scalar.activation(m.high[:, 2, :], m.staged[:, 0, :], ACT.Copy).then_inc(act_high, 1)
            act.wait_ge(pick_loaded, 16)
            nc.scalar.activation(m.pick[:], m.staged[0:64, 1, :], ACT.Copy).then_inc(act_pick, 1)
            for c in range(NCH // 2):
                act.wait_ge(pe_t, c + 1)
                nc.scalar.activation(m.gates[:, c * CH:(c + 1) * CH], ps_t[c % 2][0:64, :], ACT.Copy).then_inc(act_t, 1)

        @block.tensor
        def _(pe):
            pe.wait_ge(ready, 1)
            for c in range(NCH // 2):
                if c >= 2:
                    pe.wait_ge(act_t, c - 1)
                for k in range(KT):
                    mm = nc.tensor.transpose(ps_t[c % 2][0:64, k * P:(k + 1) * P],
                                             parts[:, c, k].rearrange("p a e -> p (a e)"), m.ident[:])
                mm.then_inc(pe_t, 1)

        @block.vector
        def _(dve):
            done = [0]

            def then(ins):
                done[0] += 1
                ins.then_inc(step, 1)
                dve.wait_ge(step, done[0])

            def pick(scores, chosen):
                then(nc.vector.tensor_reduce(red[:], scores[:], AX.X, ALU.max))
                then(nc.vector.tensor_tensor(key[:], scores[:], over(red), ALU.is_equal))
                then(nc.vector.tensor_tensor(key[:], key[:], rank, ALU.mult))
                then(nc.vector.tensor_reduce(inv[:], key[:], AX.X, ALU.max))
                then(nc.vector.tensor_tensor(chosen[:], key[:], over(inv), ALU.is_equal))

            nc.vector.memset(parts[:], 0.0)
            then(nc.vector.tensor_copy(logits[:], m.logits[:].rearrange("p (t e) -> p t e", e=E)))
            pick(logits, first)
            nc.vector.tensor_tensor(work[:], logits[:], over(red), ALU.subtract).then_inc(exp_in, 1)
            dve.wait_ge(exp_in, 1)
            then(nc.vector.scalar_tensor_tensor(logits[:], first[:], -3e38, logits[:], ALU.mult, ALU.add))
            pick(logits, second)
            then(nc.vector.tensor_tensor(first[:], first[:], second[:], ALU.add))
            dve.wait_ge(exp_out, 1)
            then(nc.vector.tensor_reduce(red[:], prob[:], AX.X, ALU.add))
            then(nc.vector.reciprocal(inv[:], red[:]))
            then(nc.vector.tensor_tensor(prob[:], prob[:], over(inv), ALU.mult))
            then(nc.vector.tensor_tensor(prob[:], prob[:], first[:], ALU.mult))
            then(nc.vector.tensor_reduce(red[:], prob[:], AX.X, ALU.add))
            then(nc.vector.tensor_scalar(red[:], red[:], 1e-20, None, ALU.add))
            then(nc.vector.reciprocal(inv[:], red[:]))
            then(nc.vector.tensor_tensor(prob[:], prob[:], over(inv), ALU.mult))
            then(nc.vector.tensor_copy(high[:], prob[:]))
            for q in range(2):
                nc.vector.tensor_copy(parts[:, :, :, q, 0:E], pairs_high[:, :, q])
                ins = nc.vector.tensor_tensor(parts[:, :, :, q, E:2 * E], pairs[:, :, q], pairs_high[:, :, q], ALU.subtract)
            ins.then_inc(ready, 1)


def run_experts(nc, m):
    LAG, RING = 3, 4
    with ExitStack() as ctx:
        sb = lambda name, shape, dt=F32: ctx.enter_context(nc.sbuf_tensor("ex_" + name, shape, dt))
        sem = lambda name: ctx.enter_context(nc.semaphore("ex_" + name))
        m.gates, m.pick = sb("gates", [64, T // 2]), sb("pick", [64, NHC * P], F32R)
        m.high, m.low = sb("w_high", [P, 3, NHC * P], F32R), sb("w_low", [P, 3, NHC * P], F32R)
        with ExitStack() as before:
            m.staged = before.enter_context(nc.sbuf_tensor("staged", [P, 2, NHC * P], F32))
            m.logits = before.enter_context(nc.sbuf_tensor("logits", [P, CH], F32))
            run_norm_phase(nc, m, EXPERTS_IN)
            run_gate(nc, m)
        x_high, x_low = sb("x_high", [P, 2, CH], F32R), sb("x_low", [P, 2, CH], F32R)
        gate = sb("gate", [64, CH], F32R)
        act_s, gated, full = sb("act_s", [P, 2, CH]), sb("gated", [P, 2, CH]), sb("full", [P, 2, CH])
        hid_high, hid_low = sb("hid_high", [P, RING, CH], F32R), sb("hid_low", [P, RING, CH], F32R)
        psum = lambda name: [ctx.enter_context(nc.psum_tensor(f"ex_{name}{k}", [P, CH], F32)) for k in range(2)]
        ps_1, ps_3, ps_g, ps_y = psum("ps_1"), psum("ps_3"), psum("ps_g"), psum("ps_y")
        dve_xh, dve_xl, pe_1, pe_g, act_1, dve_u, dve_h, act_hh, pool_hl, pe_y = (sem(k) for k in (
            "dve_xh", "dve_xl", "pe_1", "pe_g", "act_1", "dve_u", "dve_h", "act_hh", "pool_hl", "pe_y"))
        block = ctx.enter_context(nc.Block())
        slot = lambda p, j: (NHC * p + j) % RING

        def product(out, weight, w, high, low, start=True, stop=True):
            nc.tensor.matmul(out, m.high[:, weight, w], high, start=start, stop=False)
            nc.tensor.matmul(out, m.high[:, weight, w], low, start=False, stop=False)
            return nc.tensor.matmul(out, m.low[:, weight, w], high, start=False, stop=stop)

        @block.tensor
        def _(pe):
            def down(i, p, j):
                pe.wait_ge(pool_hl, NHC * i + j + 1)
                mm = product(ps_y[p][:], 2, slice(j * D, (j + 1) * D), hid_high[:, slot(p, j), :], hid_low[:, slot(p, j), :],
                             start=(j == 0), stop=(j == NHC - 1))
                if j == NHC - 1:
                    mm.then_inc(pe_y, 1)

            def turn(pair, p, before=True):
                i = 2 * pair + p
                pe.wait_ge(dve_xl, i + 1)
                for j in range(NHC):
                    if before or j >= 2:
                        pe.wait_ge(dve_h, NHC * i + j - 1)
                    w = slice(j * P, (j + 1) * P)
                    product(ps_1[j % 2][:], 0, w, x_high[:, p, :], x_low[:, p, :]).then_inc(pe_1, 1)
                    product(ps_3[j % 2][:], 1, w, x_high[:, p, :], x_low[:, p, :])
                    nc.tensor.matmul(ps_g[j % 2][:], m.pick[32 * p:32 * p + 2 * E, w], gate[32 * p:32 * p + 2 * E, :], start=True, stop=True).then_inc(pe_g, 1)
                    if j >= LAG:
                        down(i, p, j - LAG)
                    elif before:
                        down(i - 1, 1 - p, j + NHC - LAG)

            turn(0, 0, before=False)
            turn(0, 1)
            with pe.Fori(1, NCH // 2) as pair:
                turn(pair, 0)
                turn(pair, 1)
            for j in range(NHC - LAG, NHC):
                down(NCH - 1, 1, j)

        @block.scalar
        def _(act):
            def high_part(n, p, j):
                act.wait_ge(dve_h, n + 1)
                nc.scalar.activation(hid_high[:, slot(p, j), :], full[:, j % 2, :], ACT.Copy).then_inc(act_hh, 1)

            def turn(i, p, before=True):
                for j in range(NHC):
                    n = NHC * i + j
                    act.wait_ge(pe_1, n + 1)
                    nc.scalar.activation(act_s[:, j % 2, :], ps_1[j % 2][:], ACT.Silu).then_inc(act_1, 1)
                    if j:
                        high_part(n - 1, p, j - 1)
                    elif before:
                        high_part(n - 1, 1 - p, NHC - 1)

            turn(0, 0, before=False)
            turn(1, 1)
            with act.Fori(2, NCH - 1, 2) as i:
                turn(i, 0)
                turn(i + 1, 1)
            high_part(NHC * NCH - 1, 1, NHC - 1)

        @block.gpsimd
        def _(pool):
            def turn(i, p):
                for j in range(NHC):
                    pool.wait_ge(act_hh, NHC * i + j + 1)
                    nc.gpsimd.tensor_tensor(hid_low[:, slot(p, j), :], full[:, j % 2, :], hid_high[:, slot(p, j), :].bitcast(F32),
                                            ALU.subtract).then_inc(pool_hl, 1)

            with pool.Fori(0, NCH - 1, 2) as i:
                turn(i, 0)
                turn(i + 1, 1)

        @block.vector
        def _(dve):
            def split(pair, p):
                i = 2 * pair + p
                rows = slice(32 * p, 32 * p + 2 * E)
                nc.vector.tensor_copy(gate[rows, :], m.gates[rows, bass.ds(pair * CH, CH)])
                x = m.XB[:, bass.ds(i * CH, CH)]
                nc.vector.tensor_copy(x_high[:, p, :], x).then_inc(dve_xh, 1)
                dve.wait_ge(dve_xh, i + 1)
                nc.vector.tensor_tensor(x_low[:, p, :], x, x_high[:, p, :].bitcast(F32), ALU.subtract).then_inc(dve_xl, 1)

            def add(i, p):
                dve.wait_ge(pe_y, i + 1)
                for b in range(2):
                    x = m.X[:, bass.ds(i * CH + b * S, S)]
                    nc.vector.scalar_tensor_tensor(x, ps_y[p][:, b * S:(b + 1) * S], m.mod[:, 0, 5, bass.ds(i * 2 + b, 1)],
                                                   x, ALU.mult, ALU.add)

            def turn(pair, p, before=True, after=True):
                i = 2 * pair + p
                for j in range(NHC):
                    n = NHC * i + j
                    dve.wait_ge(act_1, n + 1)
                    dve.wait_ge(pe_g, n + 1)
                    nc.vector.tensor_tensor(gated[:, j % 2, :], ps_3[j % 2][:], act_s[:, j % 2, :], ALU.mult).then_inc(dve_u, 1)
                    dve.wait_ge(dve_u, n + 1)
                    if before or j >= 2:
                        dve.wait_ge(pool_hl, n - 1)
                    nc.vector.tensor_tensor(full[:, j % 2, :], ps_g[j % 2][:], gated[:, j % 2, :], ALU.mult).then_inc(dve_h, 1)
                    if before and j == LAG + 2:
                        add(i - 1, 1 - p)
                    if after and j == NHC // 2:
                        split(pair + p, 1 - p)

            split(0, 0)
            turn(0, 0, before=False)
            turn(0, 1)
            with dve.Fori(1, NCH // 2 - 1) as pair:
                turn(pair, 0)
                turn(pair, 1)
            turn(NCH // 2 - 1, 0)
            turn(NCH // 2 - 1, 1, after=False)
            add(NCH - 1, 1)


def run_l1_blocks(nc, m):
    with ExitStack() as ctx:
        sb = lambda name, shape, dt=F32: ctx.enter_context(nc.sbuf_tensor(name, shape, dt))
        sem = lambda name: ctx.enter_context(nc.semaphore(name))
        banks = [ctx.enter_context(nc.psum_tensor(f"blk_bank{k}", [P, CH], F32)) for k in range(8)]
        ps_q, ps_k, ps_v = banks[0:4], banks[4:6], banks[6:8]
        ps_o, ps_y1t, ps_z1t, ps_h, ps_f, ps_y2t, ps_z2t = (
            banks[0], banks[1], banks[2], banks[3:5], banks[5], banks[6], banks[7])

        wa = sb("wa", [P, WA_COLS])
        wb = sb("wb", [P, WB_COLS])
        w_o, w_1, w_2 = wb[:, 0:D], wb[:, D:D + FF], wb[:, D + FF:D + 2 * FF]
        bias_b = wb[:, D + 2 * FF:WB_COLS]
        b_o, ln1_s, ln1_b = (bias_b[:, k:k + 1] for k in range(3))
        b_1 = [bias_b[:, 3 + j:4 + j] for j in range(4)]
        b_2, ln2_s, ln2_b = (bias_b[:, 7 + k:8 + k] for k in range(3))
        b_q, b_k, b_v = (wa[:, 3 * D + k:3 * D + k + 1] for k in range(3))
        b_q1 = sb("b_q1", [P, 1])
        t_q, c_k, t_k = sb("t_q", [P, 2, CH]), sb("c_k", [P, 2, CH]), sb("t_k", [P, 4, CH])
        e_q, e_k = sb("e_q", [P, 2, CH]), sb("e_k", [P, 2, CH])
        q_f, k_f = sb("q_f", [P, 2, CH]), sb("k_f", [P, CH])
        kv_prod = sb("kv_prod", [P, CH])
        ksum, kvsum, ks_inv = sb("ksum", [P, 2]), sb("kvsum", [P, 2]), sb("ks_inv", [P, 2])
        ks_pos = sb("ks_pos", [P, 2])
        ks_eps, kvr, kvr_neg = sb("ks_eps", [P, 2, 2]), sb("kvr", [P, 2, 2]), sb("kvr_neg", [P, 2, 2])
        ln_t, delta = sb("ln_t", [P, 2, CH]), sb("delta", [P, 2, CH])
        g1, g2, y1, y2, z1, z2 = (sb(k, [P, CH]) for k in ("g1", "g2", "y1", "y2", "z1", "z2"))
        x1, h = sb("x1", [P, 2, CH]), sb("h", [P, 4, CH])
        ln1, ln2 = LnBuffers(sb, "blk1"), LnBuffers(sb, "blk2")

        wa_loaded, wb_loaded = sem("wa_loaded"), sem("wb_loaded")
        pe_q, pe_k, pe_v, dve_cq, pool_rq, pool_ck, act_tk, act_eq, act_ek, act_ln, act_delta, dve_qk, dve_kv, dve_v = (
            sem(k) for k in ("pe_q", "pe_k", "pe_v", "dve_cq", "pool_rq", "pool_ck", "act_tk", "act_eq", "act_ek", "act_ln",
                             "act_delta", "dve_qk", "dve_kv", "dve_v"))
        dve_b1, dve_small, pool_go = sem("dve_b1"), sem("dve_small"), sem("pool_go")
        pe_o, pe_y1t, pe_z1t, pe_h, pe_f, pe_y2t, pe_z2t = (sem(k) for k in (
            "pe_o", "pe_y1t", "pe_z1t", "pe_h", "pe_f", "pe_y2t", "pe_z2t"))
        act_g1, act_x1, act_h, act_g2, act_xb = (sem(k) for k in (
            "act_g1", "act_x1", "act_h", "act_g2", "act_xb"))
        dve_y1, dve_z1, dve_y2, dve_z2, chain1, chain2, var1, var2 = (sem(k) for k in (
            "dve_y1", "dve_z1", "dve_y2", "dve_z2", "chain1", "chain2", "var1", "var2"))
        rstd1, rstd2 = sem("rstd1"), sem("rstd2")
        block = ctx.enter_context(nc.Block())
        XB, VT = m.XB, m.VT
        FREE4, FREE2 = 4, 2

        def steps(eng, blk, lags):
            def step(i, k):
                for part, lag in lags:
                    if not isinstance(i, int) or 0 <= i - lag < NCH:
                        part(blk, i - lag, (k - lag) % 4)

            for i in range(4):
                step(i, i)
            with eng.Fori(4, NCH - 3, 4) as i:
                for k in range(4):
                    step(i + k, k)
            for i in range(NCH, NCH + 5):
                step(i, i)

        @block.sync
        def _(sp):
            with sp.Fori(0, BLOCKS) as blk:
                sp.wait_ge(dve_v, blk * NCH + FREE2)
                sp.dma_start(wa[:], m.dram["wa"][bass.ds(blk, 1)].rearrange("a p n -> (a p) n")).then_inc(wa_loaded, 16)
                sp.wait_ge(act_xb, blk * NCH + NCH)
                sp.dma_start(wb[:], m.dram["wb"][bass.ds(blk, 1)].rearrange("a p n -> (a p) n")).then_inc(wb_loaded, 16)

        @block.tensor
        def _(pe):
            def project_q(blk, c, k):
                n = blk * NCH + c
                if isinstance(c, int) and c == 0:
                    pe.wait_ge(wa_loaded, blk * 16 + 16)
                pe.wait_ge(act_xb, n + 1)
                pe.wait_ge(dve_qk, n + 1)
                nc.tensor.matmul(ps_q[k][:], wa[:, 0:D], XB[:, bass.ds(c * CH, CH)], start=True, stop=True).then_inc(pe_q, 1)

            def project_k(blk, c, k):
                n = blk * NCH + c
                pe.wait_ge(act_tk, n + 1)
                nc.tensor.matmul(ps_k[k % 2][:], wa[:, D:2 * D], XB[:, bass.ds(c * CH, CH)], start=True, stop=True).then_inc(pe_k, 1)

            def project_v(blk, c, k):
                n = blk * NCH + c
                if isinstance(c, int) and c < 2:
                    pe.wait_ge(act_xb, n - c + NCH)
                pe.wait_ge(dve_kv, n - 2 + 1 + FREE4)
                nc.tensor.matmul(ps_v[k % 2][:], wa[:, 2 * D:3 * D], XB[:, bass.ds(c * CH, CH)], start=True, stop=True).then_inc(pe_v, 1)

            def turn(blk, i, p, first=True, mid=True, last=True):
                n = blk * NCH + i
                if mid:
                    pe.wait_ge(dve_z1, n)
                    transpose_tiles(nc, ps_z1t, z1, m.ident).then_inc(pe_z1t, 1)
                if first:
                    nc.tensor.matmul(ps_o[:], w_o, VT[:, bass.ds(i * CH, CH)], start=True, stop=True).then_inc(pe_o, 1)
                if last:
                    pe.wait_ge(dve_y2, n - 1)
                    transpose_tiles(nc, ps_y2t, y2, m.ident).then_inc(pe_y2t, 1)
                if mid:
                    pe.wait_ge(act_x1, n)
                    for j in range(4):
                        if j >= 2:
                            pe.wait_ge(act_h, 4 * n - 5 + j)
                        nc.tensor.matmul(ps_h[j % 2][:], w_1[:, j * D:(j + 1) * D], x1[:, 1 - p, :],
                                         start=True, stop=True).then_inc(pe_h, 1)
                if first:
                    pe.wait_ge(dve_y1, n + 1)
                    transpose_tiles(nc, ps_y1t, y1, m.ident).then_inc(pe_y1t, 1)
                if last:
                    pe.wait_ge(dve_z2, n - 1)
                    pe.wait_ge(act_xb, n - 2 + NCH)
                    transpose_tiles(nc, ps_z2t, z2, m.ident).then_inc(pe_z2t, 1)
                if mid:
                    for j in range(4):
                        pe.wait_ge(act_h, 4 * n - 3 + j)
                        mm = nc.tensor.matmul(ps_f[:], w_2[:, j * D:(j + 1) * D], h[:, j, :], start=(j == 0), stop=(j == 3))
                    mm.then_inc(pe_f, 1)

            with pe.Fori(0, BLOCKS) as blk:
                steps(pe, blk, ((project_q, 0), (project_k, 0), (project_v, 1)))
                pe.wait_ge(wb_loaded, blk * 16 + 16)
                pe.wait_ge(dve_v, blk * NCH + NCH + FREE2)
                turn(blk, 0, 0, mid=False, last=False)
                turn(blk, 1, 1, last=False)
                with pe.Fori(2, NCH - 1, 2) as i:
                    turn(blk, i, 0)
                    turn(blk, i + 1, 1)
                turn(blk, NCH, 0, first=False)
                turn(blk, NCH + 1, 1, first=False, mid=False)

        @block.scalar
        def _(act):
            act.sem_inc(act_xb, NCH)

            act.sem_inc(act_tk, FREE2)
            act.sem_inc(act_eq, FREE2)
            act.sem_inc(act_ek, FREE2)
            act.sem_inc(act_ln, FREE2)

            def take_k(blk, c, k):
                n = blk * NCH + c
                act.wait_ge(pe_k, n + 1)
                act.wait_ge(dve_kv, n + 1)
                nc.scalar.activation(t_k[:, k, :], ps_k[k % 2][:], ACT.Identity, bias=b_k).then_inc(act_tk, 1)

            def exp_q(blk, c, k):
                n = blk * NCH + c
                act.wait_ge(dve_cq, n + 1)
                act.wait_ge(dve_qk, n - 2 + 1 + FREE4)
                nc.scalar.activation(e_q[:, k % 2, :], t_q[:, k % 2, :], ACT.Exp).then_inc(act_eq, 1)

            def exp_k(blk, c, k):
                n = blk * NCH + c
                act.wait_ge(pool_ck, n + 1)
                nc.scalar.activation(e_k[:, k % 2, :], c_k[:, k % 2, :], ACT.Exp).then_inc(act_ek, 1)

            def deltas(blk, c, k):
                n = blk * NCH + c
                p = k % 2
                act.wait_ge(dve_kv, n + 1 + FREE4)
                for b in range(2):
                    s = slice(b * S, (b + 1) * S)
                    ins = nc.scalar.activation(ln_t[:, p, s], q_f[:, p, s], ACT.Ln, bias=1.0, scale=ks_eps[:, p, b:b + 1])
                ins.then_inc(act_ln, 1)
                act.wait_ge(act_ln, n + 1 + FREE2)
                act.wait_ge(dve_v, n + 1)
                nc.scalar.activation(delta[:, p, :], ln_t[:, p, :], ACT.Exp, scale=-1.0).then_inc(act_delta, 1)

            def turn(blk, i, p, first=True, mid=True, last=True):
                n = blk * NCH + i
                if mid:
                    act.wait_ge(pe_z1t, n)
                    nc.scalar.activation(x1[:, 1 - p, :], ps_z1t[:], ACT.Identity,
                                         bias=ln1_b, scale=ln1_s).then_inc(act_x1, 1)
                if first:
                    act.wait_ge(pe_o, n + 1)
                    nc.scalar.activation(g1[:], ps_o[:], ACT.Gelu_apprx_tanh, bias=b_o).then_inc(act_g1, 1)
                if mid:
                    for j in range(4):
                        act.wait_ge(pe_h, 4 * n - 3 + j)
                        nc.scalar.activation(h[:, j, :], ps_h[j % 2][:], ACT.Gelu_apprx_tanh, bias=b_1[j]).then_inc(act_h, 1)
                if last:
                    act.wait_ge(pe_z2t, n - 1)
                    nc.scalar.activation(XB[:, bass.ds((i - 2) * CH, CH)], ps_z2t[:], ACT.Identity,
                                         bias=ln2_b, scale=ln2_s).then_inc(act_xb, 1)
                if mid:
                    act.wait_ge(pe_f, n)
                    nc.scalar.activation(g2[:], ps_f[:], ACT.Gelu_apprx_tanh, bias=b_2).then_inc(act_g2, 1)

            with act.Fori(0, BLOCKS) as blk:
                nc.scalar.preload_act_table_set("natural_log_exp_and_others")
                steps(act, blk, ((take_k, 0), (exp_q, 1), (exp_k, 1), (deltas, 3)))
                nc.scalar.preload_act_table(ACT.Gelu_apprx_tanh)
                turn(blk, 0, 0, mid=False, last=False)
                turn(blk, 1, 1, last=False)
                with act.Fori(2, NCH - 1, 2) as i:
                    turn(blk, i, 0)
                    turn(blk, i + 1, 1)
                turn(blk, NCH, 0, first=False)
                turn(blk, NCH + 1, 1, first=False, mid=False)

        @block.gpsimd
        def _(pool):
            def rstds(blk, i, one, two):
                n = blk * NCH + i
                if two:
                    pool.wait_ge(var2, n - 1)
                    nc.gpsimd.tensor_tensor(ln2.rstd[:], ln2.var[:], m.neg_half[:], ALU.pow).then_inc(rstd2, 1)
                if one:
                    pool.wait_ge(var1, n + 1)
                    nc.gpsimd.tensor_tensor(ln1.rstd[:], ln1.var[:], m.neg_half[:], ALU.pow).then_inc(rstd1, 1)

            def clamp_k(blk, c, k):
                n = blk * NCH + c
                pool.wait_ge(act_tk, n + 1 + FREE2)
                pool.wait_ge(act_ek, n + 1)
                pool.sem_inc(pool_go, 1)
                nc.gpsimd.tensor_scalar(c_k[:, k % 2, :], t_k[:, k, :], 0.0, None, ALU.min).then_inc(pool_ck, 1)

            def round_q(blk, c, k):
                n = blk * NCH + c
                pool.wait_ge(act_eq, n + 1 + FREE2)
                pool.sem_inc(pool_go, 1)
                nc.gpsimd.tensor_scalar(e_q[:, k % 2, :], e_q[:, k % 2, :], 1.0, -1.0, ALU.mult, ALU.add).then_inc(pool_rq, 1)
                pool.wait_ge(pool_rq, 2 * n + 1)
                pool.sem_inc(pool_go, 1)
                nc.gpsimd.tensor_scalar(e_q[:, k % 2, :], e_q[:, k % 2, :], 1.0, 1.0, ALU.mult, ALU.add).then_inc(pool_rq, 1)

            with pool.Fori(0, BLOCKS) as blk:
                steps(pool, blk, ((round_q, 1), (clamp_k, 0)))
                rstds(blk, 0, True, False)
                rstds(blk, 1, True, False)
                with pool.Fori(2, NCH) as i:
                    rstds(blk, i, True, True)
                rstds(blk, NCH, False, True)
                rstds(blk, NCH + 1, False, True)

        @block.vector
        def _(dve):
            dve.sem_inc(dve_qk, FREE4)
            dve.sem_inc(dve_kv, FREE4)
            dve.sem_inc(dve_v, FREE2)

            def clamp_q(blk, c, k):
                n = blk * NCH + c
                dve.wait_ge(pe_q, n + 1)
                dve.wait_ge(act_eq, n + 1)
                nc.vector.tensor_scalar(t_q[:, k % 2, :], ps_q[k][:], b_q, 0.0, ALU.add, ALU.min).then_inc(dve_cq, 1)

            def features(blk, c, k):
                n = blk * NCH + c
                p = k % 2
                dve.wait_ge(pool_rq, 2 * n + 2)
                dve.wait_ge(act_ln, n + 1)
                nc.vector.scalar_tensor_tensor(q_f[:, p, :], ps_q[k][:], b_q1[:], e_q[:, p, :], ALU.add, ALU.max)
                dve.wait_ge(act_ek, n + 1 + FREE2)
                for b in range(2):
                    s = slice(b * S, (b + 1) * S)
                    ins = nc.vector.scalar_tensor_tensor(k_f[:, s], t_k[:, k, s], 1.0, e_k[:, p, s],
                                                         ALU.add, ALU.max, accum_out=ksum[:, b:b + 1])
                ins.then_inc(dve_qk, 1)

            def sums(blk, c, k):
                n = blk * NCH + c
                p = k % 2
                dve.wait_ge(pe_v, n + 1)
                dve.wait_ge(dve_qk, n + 1 + FREE4)
                for b in range(2):
                    s = slice(b * S, (b + 1) * S)
                    ins = nc.vector.scalar_tensor_tensor(kv_prod[:, s], ps_v[p][:, s], b_v, k_f[:, s],
                                                         ALU.add, ALU.mult, accum_out=kvsum[:, b:b + 1])
                nc.vector.tensor_scalar(ks_eps[:, p, :], ksum[:], 1.0 / EPS_ATTN, None, ALU.mult)
                nc.vector.tensor_scalar(ks_pos[:], ksum[:], 1e-30, None, ALU.max).then_inc(dve_small, 1)
                dve.wait_ge(dve_small, 3 * n + 1)
                nc.vector.reciprocal(ks_inv[:], ks_pos[:]).then_inc(dve_small, 1)
                dve.wait_ge(dve_small, 3 * n + 2)
                dve.wait_ge(dve_v, n + 1)
                nc.vector.tensor_tensor(kvr[:, p, :], kvsum[:], ks_inv[:], ALU.mult).then_inc(dve_small, 1)
                dve.wait_ge(dve_small, 3 * n + 3)
                nc.vector.tensor_scalar(kvr_neg[:, p, :], kvr[:, p, :], -1.0, None, ALU.mult).then_inc(dve_kv, 1)

            def values(blk, c, k):
                n = blk * NCH + c
                p = k % 2
                dve.wait_ge(act_delta, n + 1)
                for b in range(2):
                    ins = nc.vector.tensor_scalar(VT[:, bass.ds(c * CH + b * S, S)], delta[:, p, b * S:(b + 1) * S],
                                                  kvr_neg[:, p, b:b + 1], kvr[:, p, b:b + 1], ALU.mult, ALU.add)
                ins.then_inc(dve_v, 1)

            def turn(blk, i, p, first=True, mid=True, last=True):
                n = blk * NCH + i
                if last:
                    dve.wait_ge(pe_y2t, n - 1)
                    ln_stats(nc, dve, ln2, ps_y2t, chain2, n - 2, var2, EPS_BLK)
                if first:
                    dve.wait_ge(act_g1, n + 1)
                    nc.vector.tensor_tensor(y1[:], g1[:], XB[:, bass.ds(i * CH, CH)], ALU.add).then_inc(dve_y1, 1)
                if last:
                    dve.wait_ge(rstd2, n - 1)
                    dve.wait_ge(pe_z2t, n - 2)
                    ln_apply(nc, ln2, z2, ps_y2t).then_inc(dve_z2, 1)
                if first:
                    dve.wait_ge(pe_y1t, n + 1)
                    ln_stats(nc, dve, ln1, ps_y1t, chain1, n, var1, EPS_BLK)
                    dve.wait_ge(rstd1, n + 1)
                    dve.wait_ge(pe_z1t, n)
                    ln_apply(nc, ln1, z1, ps_y1t).then_inc(dve_z1, 1)
                if mid:
                    dve.wait_ge(act_g2, n)
                    nc.vector.tensor_tensor(y2[:], g2[:], x1[:, 1 - p, :],
                                            ALU.add).then_inc(dve_y2, 1)

            with dve.Fori(0, BLOCKS) as blk:
                dve.wait_ge(wa_loaded, blk * 16 + 16)
                nc.vector.tensor_scalar(b_q1[:], b_q, 1.0, None, ALU.add).then_inc(dve_b1, 1)
                dve.wait_ge(dve_b1, blk + 1)
                steps(dve, blk, ((clamp_q, 0), (values, 4), (features, 2), (sums, 2)))
                turn(blk, 0, 0, mid=False, last=False)
                turn(blk, 1, 1, last=False)
                with dve.Fori(2, NCH - 1, 2) as i:
                    turn(blk, i, 0)
                    turn(blk, i + 1, 1)
                turn(blk, NCH, 0, first=False)
                turn(blk, NCH + 1, 1, first=False, mid=False)


def attention_constants():
    stack = np.zeros((P, 4, 4, P), np.float32)
    for g in range(4):
        for j in range(4):
            for dd in range(HD):
                f = (4 * g + j) * HD + dd
                for part, places in enumerate(((0, 2), (1,), (0, 1), (2,))):
                    for r in places:
                        stack[f, part, g, 32 * j + 8 * r + dd] = 1.0
    p, c = np.arange(P)[:, None], np.arange(KEYS)[None, :]
    near = np.concatenate([np.abs(c - p) <= WINDOW, np.abs(c - p - WINDOW) <= WINDOW], 1)
    masks = np.where(near, 0.0, -1e38).astype(np.float32)
    ones_rows = ((np.arange(P) % 32 == 24) | (np.arange(P) % 32 == 25)).astype(np.float32)[:, None]
    return stack.reshape(P, NSTACK * P), masks, ones_rows


def expert_selectors():
    expert = np.arange(NHC * P) // HID
    sel = (expert[None, :] == np.arange(E)[:, None]).astype(np.float32)
    sel = np.concatenate([sel, sel, np.zeros((32 - 2 * E, NHC * P), np.float32)], 0)
    return np.concatenate([sel, sel], 0)


def layout(i):
    c = lambda a: np.ascontiguousarray(a)
    col = lambda a: np.asarray(a).reshape(-1, 1)
    g = {k: np.asarray(v) for k, v in i.items()}
    a = lambda k: g["L1_attn_" + k]
    stack, masks, ones_rows = attention_constants()
    bq = g["L0_attn_b_qkv"]
    w_out = np.zeros((4, 32, 4, D), np.float32)
    w_out[:, 0:HD] = g["L0_attn_w_out"].reshape(4, 4, HD, D).transpose(1, 2, 0, 3)
    w_out = w_out.reshape(P, 4, D)
    per = lambda k: a(k)[:, :, None]
    return dict(
        x=c(g["L0_attn_x"].reshape(T, D).T),
        cond=c(np.stack([g["L0_c"].T, g["L1_c"].T], 1)),
        wmod=c(np.stack([g["L0_wmod"], g["L1_wmod"]], 1)),
        w_qkv=c(g["L0_attn_w_qkv"]), w_out=w_out,
        misc=c(np.concatenate([col(bq[0:D]), col(bq[D:2 * D]), col(g["L0_attn_b_out"]), col(g["L1_ffn_b"]), ones_rows,
                               np.broadcast_to(bq[2 * D:], (P, D)),
                               np.broadcast_to(np.arange(E, 0, -1, dtype=np.float32), (P, E))], 1)),
        stack=stack, masks=masks, ident=np.eye(P, dtype=np.float32), experts=expert_selectors(),
        w_gate=c(g["L0_ffn_Wg"].T),
        w1=c(g["L0_ffn_W1"].reshape(E * HID, D).T), w3=c(g["L0_ffn_W3"].reshape(E * HID, D).T),
        w2=c(g["L0_ffn_W2"].transpose(0, 2, 1).reshape(NHC, P, D).transpose(1, 0, 2).reshape(P, NHC * D)),
        down_t=c(g["L1_ffn_lora_down"].T), down_aux=c(g["L1_ffn_down_aux"]),
        up_t=c(g["L1_ffn_lora_up"].T), up_aux_t=c(g["L1_ffn_up_aux"].T), w_t=c(g["L1_ffn_W"].T),
        wa=c(np.concatenate([a("Wq"), a("Wk"), a("Wv"), per("bq"), per("bk"), per("bv")], 2)),
        wb=c(np.concatenate([
            a("Wo"), a("W1"), a("W2").reshape(BLOCKS, 4, P, D).transpose(0, 2, 1, 3).reshape(BLOCKS, P, 4 * D),
            per("bo"), per("ln1_s"), per("ln1_b"), a("b1").reshape(BLOCKS, 4, P).transpose(0, 2, 1),
            per("b2"), per("ln2_s"), per("ln2_b")], 2)),
    )


def build(nc, dram, out):
    m = Chip()
    m.dram, m.out = dram, out
    with ExitStack() as ctx:
        sb = lambda name, shape, dt=F32: ctx.enter_context(nc.sbuf_tensor(name, shape, dt))
        m.X, m.XB = sb("X", [P, T]), sb("XB", [P, T])
        m.ident, m.neg_half, m.misc = sb("ident", [P, P]), sb("neg_half", [P, KT]), sb("misc_sb", [P, 5 + D + E])
        m.mod, m.w_ffn = sb("mod", [P, 2, 6, B]), sb("w_ffn", [P, D])
        m.gain_bout, m.gain_bffn, m.bq_scaled = sb("gain_bout", [P, B]), sb("gain_bffn", [P, B]), sb("bq_scaled", [P, 1])
        m.w_gate = sb("w_gate", [P, E])
        with ExitStack() as l0:
            sb0 = lambda name, shape, dt=F32: l0.enter_context(nc.sbuf_tensor(name, shape, dt))
            with ExitStack() as att:
                sba = lambda name, shape, dt=F32: att.enter_context(nc.sbuf_tensor(name, shape, dt))
                m.k_all, m.v_all, m.w_qkv, m.w_out = sba("k_all", [P, T]), sba("v_all", [P, T]), sba("w_qkv_sb", [P, 3 * D]), sba("w_out_sb", [P, 4, D])
                m.ident_b, m.masks = sba("ident_b", [P, P], BF16), sba("masks_sb", [P, 2 * KEYS], BF16)
                m.stack = sba("stack_sb", [P, NSTACK, P], F32R)
                m.m_cols = sba("m_cols", [P, 2, 2, P])
                m.v_aug, m.ones_v = sba("v_aug", [P, 2, 2, H, 32]), sba("ones_v", [P, 32])
                run_setup(nc, m)
                run_attention_inputs(nc, m)
                run_attention(nc, m)
            run_experts(nc, m)
        run_norm_phase(nc, m, BLOCKS_IN)
        m.VT = sb("VT", [P, T])
        run_l1_blocks(nc, m)
        run_norm_phase(nc, m, LAST)


def kernel(**inputs):
    from concourse import bacc
    from concourse.bass_utils import run_bass_kernel_spmd

    nc = bacc.Bacc("TRN2", target_bir_lowering=False, num_devices=1)
    arrays = {"in_" + k: v for k, v in layout(inputs).items()}
    dram = {k[3:]: nc.dram_tensor(k, v.shape, F32, kind="ExternalInput").ap() for k, v in arrays.items()}
    out = nc.dram_tensor("out", (P, T), F32, kind="ExternalOutput").ap()
    build(nc, dram, out)
    result = run_bass_kernel_spmd(nc, [arrays], core_ids=[0])
    return np.ascontiguousarray(result.results[0]["out"].T).reshape(B, S, D)
```
